# Optimizing a Trainium2 kernel written in Bass

```python
import numpy as np
import jax
import jax.numpy as jnp

def _softmax(x, axis=-1):
    return jax.nn.softmax(x, axis=axis)

def _gelu(x):
    return jax.nn.gelu(x, approximate=True)

def _silu(x):
    return jax.nn.silu(x)

def _sigmoid(x):
    return jax.nn.sigmoid(x)

def _layernorm(x, axis=-1, eps=1e-05):
    m = jnp.mean(x, axis=axis, keepdims=True)
    v = jnp.var(x, axis=axis, keepdims=True)
    return (x - m) / jnp.sqrt(v + eps)

def _scatter_add(tgt, idx, src, axis=0):
    return tgt.at[idx].add(src)

def _segment_sum(src, seg, n):
    return jax.ops.segment_sum(src, seg, n)
kernel_name = 'mk_rec_standalone_d1_rec_r8_d2cd60'

def setup_inputs(seed: int=0):
    np.random.seed(seed)
    _w = jnp.asarray

    def _rec_inputs():
        import jax
        import jax.numpy as jnp
        _rk = jax.random.key(seed)
        r_inputs = -7.10856e-05 + 0.999911 * jax.random.normal(jax.random.fold_in(_rk, 1), (2048, 128, 128), jnp.float32)
        return r_inputs
    r_inputs = _rec_inputs()

    def _L0_rec_setup():
        import jax, jax.numpy as jnp
        import numpy as np
        BS, F, E = (512, 128, 128)
        A, NH = (128, 2)
        key = jax.random.key(seed)
        ks = jax.random.split(key, 12)
        s = 0.02
        return {'inputs': jax.random.normal(ks[0], (BS, F, E), dtype=jnp.float32), 'unary_w': jax.random.normal(ks[1], (NH, E), dtype=jnp.float32) * s, 'unary_b': jax.random.normal(ks[2], (NH,), dtype=jnp.float32) * s, 'wq_w': jax.random.normal(ks[3], (A, E), dtype=jnp.float32) * s, 'wq_b': jax.random.normal(ks[4], (A,), dtype=jnp.float32) * s, 'wk_w': jax.random.normal(ks[5], (A, E), dtype=jnp.float32) * s, 'wk_b': jax.random.normal(ks[6], (A,), dtype=jnp.float32) * s, 'wv_w': jax.random.normal(ks[7], (A, E), dtype=jnp.float32) * s, 'wv_b': jax.random.normal(ks[8], (A,), dtype=jnp.float32) * s, 'res_w': jax.random.normal(ks[9], (E, E), dtype=jnp.float32) * s, 'res_b': jax.random.normal(ks[10], (E,), dtype=jnp.float32) * s}
    _L0_rec_all = _L0_rec_setup()
    _L0_rec_in = {k: v for k, v in _L0_rec_all.items() if k in ('unary_w', 'unary_b', 'wq_w', 'wq_b', 'wk_w', 'wk_b', 'wv_w', 'wv_b', 'res_w', 'res_b')}
    del _L0_rec_all
    return {'r_inputs': r_inputs, 'L0_rec_unary_w': _L0_rec_in['unary_w'], 'L0_rec_unary_b': _L0_rec_in['unary_b'], 'L0_rec_wq_w': _L0_rec_in['wq_w'], 'L0_rec_wq_b': _L0_rec_in['wq_b'], 'L0_rec_wk_w': _L0_rec_in['wk_w'], 'L0_rec_wk_b': _L0_rec_in['wk_b'], 'L0_rec_wv_w': _L0_rec_in['wv_w'], 'L0_rec_wv_b': _L0_rec_in['wv_b'], 'L0_rec_res_w': _L0_rec_in['res_w'], 'L0_rec_res_b': _L0_rec_in['res_b']}

def reference(r_inputs, L0_rec_unary_w, L0_rec_unary_b, L0_rec_wq_w, L0_rec_wq_b, L0_rec_wk_w, L0_rec_wk_b, L0_rec_wv_w, L0_rec_wv_b, L0_rec_res_w, L0_rec_res_b):
    import jax
    import jax.numpy as jnp

    def _L0_rec_ref(inputs, unary_w, unary_b, wq_w, wq_b, wk_w, wk_b, wv_w, wv_b, res_w, res_b):
        import jax, jax.numpy as jnp
        import numpy as np
        BS, F, E = (512, 128, 128)
        A, NH = (128, 2)
        bs = inputs.shape[0]
        n_head = unary_w.shape[0]
        attn_dim = wq_w.shape[0]
        dph = attn_dim // n_head
        unary = inputs @ unary_w.T + unary_b
        unary_weight = jax.nn.softmax(unary, axis=1).reshape(bs * n_head, -1, 1)
        query = (inputs @ wq_w.T + wq_b).reshape(bs * n_head, -1, dph)
        key = (inputs @ wk_w.T + wk_b).reshape(bs * n_head, -1, dph)
        value = (inputs @ wv_w.T + wv_b).reshape(bs * n_head, -1, dph)
        mu_query = query - query.mean(axis=1, keepdims=True)
        mu_key = key - key.mean(axis=1, keepdims=True)
        pair_weight = jnp.einsum('bnd,bmd->bnm', mu_query, mu_key) / jnp.sqrt(jnp.asarray(dph, dtype=inputs.dtype))
        pair_weight = jax.nn.softmax(pair_weight, axis=2)
        attn = unary_weight + pair_weight
        output = (attn @ value).reshape(bs, -1, attn_dim)
        output = output + inputs @ res_w.T + res_b
        return output
    y = _L0_rec_ref(r_inputs, L0_rec_unary_w, L0_rec_unary_b, L0_rec_wq_w, L0_rec_wq_b, L0_rec_wk_w, L0_rec_wk_b, L0_rec_wv_w, L0_rec_wv_b, L0_rec_res_w, L0_rec_res_b)
    return y

_drawn_inputs = setup_inputs


def setup_inputs(seed=0):
    import zlib

    import numpy as np

    out = dict(_drawn_inputs(seed))
    spreads = {}
    factors = {'L0_rec_unary_b': 200.0,
     'L0_rec_wq_w': 8.0,
     'L0_rec_wq_b': 8.0,
     'L0_rec_wk_w': 8.0,
     'L0_rec_wk_b': 8.0}
    for name, (base, spread) in spreads.items():
        noise = np.random.default_rng([zlib.crc32(name.encode()), seed]).standard_normal(out[name].shape)
        drawn = base * np.exp(spread * noise) if base else spread * noise
        out[name] = jnp.asarray(drawn.astype(out[name].dtype))
    for name, factor in factors.items():
        out[name] = (out[name] * factor).astype(out[name].dtype)
    return out
```

```python
from contextlib import ExitStack

import concourse.bass as bass
from concourse import mybir

F32 = mybir.dt.float32
ALU = mybir.AluOpType
ACT = mybir.ActivationFunctionType
AX = mybir.AxisListType

GROUP = 4
SPAN = 4
UNROLL = 8
QUERY, KEY = 0, 1


def attention_kernel(nc, x, unary_w, unary_b, wq_w, wq_b, wk_w, wk_b, wv_w, wv_b, res_w, res_b, out):
    BS, F, E = x.shape
    A = wq_w.shape[0]
    NH = unary_w.shape[0]
    DPH = A // NH
    FH = F // NH
    N = NH * FH
    assert NH == 2 and F == E == A == N == 128
    GROUPS = BS // GROUP
    SPAN_BS = SPAN * GROUP
    VU = DPH + 1
    INV_SQRT = float(DPH) ** -0.5
    LAST = GROUPS // UNROLL - 1
    assert GROUPS % UNROLL == 0 and INV_SQRT == 0.125

    def exists(i, g):
        return not isinstance(i, int) or 0 <= UNROLL * i + g < GROUPS

    def count(i, g, each=1):
        return i * (UNROLL * each) + (g + 1) * each

    def spans(i, g, each=1):
        return i * (UNROLL // SPAN * each) + (g // SPAN + 1) * each

    def uses(i, g, ring, each=1):
        return i * (UNROLL // ring * each) + (g // ring + 1) * each

    def wait(eng, sem, value):
        if not isinstance(value, int) or value > 0:
            eng.wait_ge(sem, value)

    def wait_and_step(eng, sem, value, register, peeled):
        if peeled:
            eng.wait_ge(sem, value)
        else:
            eng.wait_ge(sem, register)
            eng.reg_add(register, register, 1)

    def steps(eng, step, first, last):
        for t in range(first, UNROLL):
            step(t // UNROLL, t % UNROLL)
        with eng.Fori(1, LAST) as i:
            for s in range(UNROLL):
                step(i, s)
        for t in range(UNROLL * LAST, last):
            step(t // UNROLL, t % UNROLL)

    x_groups = x.rearrange("(t b) f e -> t f b e", b=GROUP)
    out_groups = out.rearrange("(t b) f a -> t f b a", b=GROUP)

    with ExitStack() as ctx:
        def sb(name, shape):
            return ctx.enter_context(nc.sbuf_tensor(name, shape, F32))

        def bank(name):
            return ctx.enter_context(nc.psum_tensor(name, [128, 512], F32))

        def sem(name):
            return ctx.enter_context(nc.semaphore(name))

        X_RING, XT_RING, V_RING = 4, UNROLL, UNROLL

        ident = sb("ident", [128, 128])
        w_rows = sb("w_rows", [A, 4, E])
        wu_rows = sb("wu_rows", [NH, E])
        wqk = sb("wqk", [E, 2, A])
        wvu = sb("wvu", [E, NH, VU])
        wr = sb("wr", [E, A])
        w_mean = sb("w_mean", [E, 2, DPH])
        b_rows = sb("b_rows", [128, 2, NH])
        b_sum = sb("b_sum", [128, 2])
        b_half = sb("b_half", [128, 2, NH])
        b_centred = sb("b_centred", [128, 2, NH])
        bvu = sb("bvu", [128, VU])
        br = sb("br", [128, A])

        x_in = sb("x_in", [F, X_RING, GROUP, E])
        xt = sb("xt", [E, XT_RING, GROUP, F])
        xsum = sb("xsum", [E, NH, SPAN_BS])
        offset = sb("offset", [128, 2, NH, SPAN_BS])
        vu = sb("vu", [N, V_RING, GROUP, NH, VU])
        qs = sb("qs", [128, 2, GROUP, N])
        ks = sb("ks", [128, 2, GROUP, N])
        neg_max = sb("neg_max", [N, 2, NH, GROUP])
        row_sum = sb("row_sum", [N, 2, NH, GROUP])
        row_inv = sb("row_inv", [N, 2, NH, GROUP])
        attn = sb("attn", [N, 2, NH, GROUP, N])
        attn_t = sb("attn_t", [N, 2, GROUP, NH, N])
        o_sb = sb("o_sb", [F, 2, GROUP, A])
        u_neg_max = sb("u_neg_max", [SPAN_BS, NH])
        u_exp = sb("u_exp", [SPAN_BS, NH, NH, FH])
        u_sum = sb("u_sum", [SPAN_BS, NH])
        u_inv = sb("u_inv", [SPAN_BS, NH])
        u_soft = sb("u_soft", [SPAN_BS, NH, NH, FH])
        unary = sb("unary", [N, 2, NH, SPAN_BS])

        misc_bank = bank("misc_bank")
        vu_bank = bank("vu_bank")
        q_bank = bank("q_bank")
        k_bank = bank("k_bank")
        s_bank = [bank("s_bank0"), bank("s_bank1")]
        t_bank = bank("t_bank")
        o_bank = bank("o_bank")

        x_loaded = [sem(f"x_loaded{r}") for r in range(X_RING)]
        out_stored = [sem(f"out_stored{r}") for r in range(2)]
        weights_loaded = sem("weights_loaded")
        ident_zeroed = sem("ident_zeroed")
        ident_ready = sem("ident_ready")
        weights_turned = sem("weights_turned")
        constant_step = sem("constant_step")
        constants_ready = sem("constants_ready")
        xt_ready, xt_copied = sem("xt_ready"), sem("xt_copied")
        xsum_ready = sem("xsum_ready")
        mean_ready, offset_ready = sem("mean_ready"), sem("offset_ready")
        vu_ready, vu_copied = sem("vu_ready"), sem("vu_copied")
        q_ready, q_copied = sem("q_ready"), sem("q_copied")
        k_ready, k_copied = sem("k_ready"), sem("k_copied")
        s_ready = sem("s_ready")
        max_ready = sem("max_ready")
        exp_done = sem("exp_done")
        inv_ready = sem("inv_ready")
        attn_ready = sem("attn_ready")
        attn_t_ready, attn_t_copied = sem("attn_t_ready"), sem("attn_t_copied")
        o_ready, o_copied = sem("o_ready"), sem("o_copied")
        u_turned = sem("u_turned")
        u_max_ready = sem("u_max_ready")
        u_exp_done = sem("u_exp_done")
        u_inv_ready = sem("u_inv_ready")
        u_soft_ready = sem("u_soft_ready")
        unary_turned, unary_copied = sem("unary_turned"), sem("unary_copied")

        WEIGHT_DMAS = 5 + 4 + 4 + 1
        CONSTANTS = 6

        block = ctx.enter_context(nc.Block())

        @block.sync
        def _(sp):
            for n, w in enumerate((wq_w, wk_w, wv_w, res_w)):
                sp.dma_start(w_rows[:, n, :], w).then_inc(weights_loaded, 16)
            sp.dma_start(wu_rows[:, :], unary_w).then_inc(weights_loaded, 16)
            for half in range(2):
                here = slice(half * DPH, (half + 1) * DPH)
                for which, bias in ((QUERY, wq_b), (KEY, wk_b)):
                    sp.dma_start(b_rows[here, which, :], bias.rearrange("(h d) -> d h", h=NH),
                                 allow_slow_non_contiguous=True).then_inc(weights_loaded, 16)
                sp.dma_start(bvu[here, 0:DPH], wv_b[here].partition_broadcast(FH)).then_inc(weights_loaded, 16)
                sp.dma_start(bvu[here, DPH:VU], unary_b[half:half + 1].partition_broadcast(FH)).then_inc(weights_loaded, 16)
            sp.dma_start(br[:, :], res_b.partition_broadcast(F)).then_inc(weights_loaded, 16)

            def step(i, s):
                ahead = s + 2 * SPAN
                if exists(i, ahead):
                    wait(sp, xt_ready, count(i, ahead - X_RING))
                    sp.dma_start(x_in[:, ahead % X_RING, :, :], x_groups[UNROLL * i + ahead]).then_inc(
                        x_loaded[ahead % X_RING], 16)
                if exists(i, s - 2):
                    wait(sp, o_copied, count(i, s - 2))
                    sp.dma_start(out_groups[UNROLL * i + (s - 2)], o_sb[:, s % 2, :, :]).then_inc(
                        out_stored[s % 2], 16)

            steps(sp, step, -2 * SPAN, GROUPS + 2)
            for r in range(2):
                sp.wait_ge(out_stored[r], 16 * (GROUPS // 2))

        @block.gpsimd
        def _(pool):
            inv_count, unary_count = pool.alloc_register("inv_count"), pool.alloc_register("unary_count")
            pool.reg_mov(inv_count, count(1, -1, 2) - 1)
            pool.reg_mov(unary_count, spans(1, 0))
            nc.gpsimd.memset(ident[:, :], 0.0).then_inc(ident_zeroed, 1)
            pool.wait_ge(ident_zeroed, 1)
            nc.gpsimd.affine_select(out=ident[:, :], in_=ident[:, :], compare_op=ALU.not_equal, fill=1.0,
                                    base=0, pattern=[[-1, 128]], channel_multiplier=1).then_inc(ident_ready, 1)

            def step(i, s):
                c = s - 1
                if not exists(i, c):
                    return
                if c % SPAN == 0:
                    wait_and_step(pool, unary_copied, spans(i, c), unary_count, isinstance(i, int))
                for g in range(NH):
                    wait_and_step(pool, inv_ready, count(i, c, 2) - 1 + g, inv_count, isinstance(i, int))
                    for b in range(GROUP):
                        at = (c % SPAN) * GROUP + b
                        last = nc.gpsimd.tensor_scalar(
                            attn[:, c % 2, g, b, :], attn[:, c % 2, g, b, :], row_inv[:, c % 2, g, b:b + 1],
                            unary[:, c // SPAN % 2, g, at:at + 1], ALU.mult, ALU.add)
                    last.then_inc(attn_ready, 1)

            steps(pool, step, 0, GROUPS + 1)

        @block.scalar
        def _(act):
            def step(i, s):
                u, c, d = s + SPAN, s - 1, s - 2

                def attn_t_copy(half):
                    wait(act, attn_t_ready, count(i, d, 2) - 1 + half)
                    nc.scalar.copy(attn_t[:, d % 2, 2 * half:2 * half + 2, :, :].rearrange("p b g n -> p (b g n)"),
                                   t_bank[:, :]).then_inc(attn_t_copied, 1)

                def exponentials(g, batch):
                    for b in batch:
                        last = nc.scalar.activation(
                            attn[:, c % 2, g, b, :], s_bank[g][:, b * N:(b + 1) * N], ACT.Exp,
                            bias=neg_max[:, c % 2, g, b:b + 1], scale=1.0,
                            accum_out=row_sum[:, c % 2, g, b:b + 1])
                    if batch[-1] == GROUP - 1:
                        last.then_inc(exp_done, 1)

                if exists(i, u):
                    wait(act, xt_ready, count(i, u))
                    wait(act, o_ready, count(i, u - XT_RING))
                    nc.scalar.copy(xt[:, u % XT_RING, :, :].rearrange("p b f -> p (b f)"),
                                   misc_bank[:, :]).then_inc(xt_copied, 1)
                elif exists(i, d):
                    wait(act, o_ready, count(i, d - 2))
                if exists(i, c):
                    wait(act, max_ready, count(i, c, 2) - 1)
                    exponentials(0, range(0, 4))
                if exists(i, d):
                    attn_t_copy(0)
                if exists(i, c):
                    wait(act, max_ready, count(i, c, 2))
                    exponentials(1, range(0, 2))
                if exists(i, d):
                    attn_t_copy(1)
                if exists(i, c):
                    exponentials(1, range(2, 4))
                if s % SPAN == 0 and exists(i, s):
                    wait(act, u_max_ready, spans(i, s))
                    turned = misc_bank[0:SPAN_BS, 0:NH * N].rearrange("p (g h f) -> p h g f", g=NH, h=NH)
                    for h in range(NH):
                        nc.scalar.activation(u_exp[:, :, h, :], turned[:, h, :, :], ACT.Exp,
                                             bias=u_neg_max[:, h:h + 1], scale=1.0,
                                             accum_out=u_sum[:, h:h + 1]).then_inc(u_exp_done, 1)

            steps(act, step, -SPAN, GROUPS + 2)

        @block.vector
        def _(dve):
            dve.wait_ge(weights_loaded, 16 * WEIGHT_DMAS)
            dve.wait_ge(weights_turned, 2)
            wt = misc_bank[:, :].rearrange("p (w a) -> p w a", w=4)
            nc.vector.tensor_scalar(wqk[:, QUERY, :], wt[:, 0, :], INV_SQRT, None, ALU.mult).then_inc(constant_step, 1)
            nc.vector.tensor_copy(wqk[:, KEY, :], wt[:, 1, :]).then_inc(constant_step, 1)
            nc.vector.tensor_copy(wvu[:, :, 0:DPH], wt[:, 2, :].rearrange("p (h d) -> p h d", h=NH)).then_inc(constants_ready, 1)
            nc.vector.tensor_copy(wr[:, :], wt[:, 3, :]).then_inc(constants_ready, 1)
            nc.vector.tensor_copy(wvu[:, :, DPH], vu_bank[:, 0:NH]).then_inc(constants_ready, 1)
            nc.vector.tensor_tensor(b_sum[:, :], b_rows[:, :, 0], b_rows[:, :, 1], ALU.add).then_inc(constant_step, 1)
            dve.wait_ge(constant_step, 3)
            nc.vector.tensor_tensor(w_mean[:, :, :], wqk[:, :, 0:DPH], wqk[:, :, DPH:A], ALU.add).then_inc(constant_step, 1)
            for h in range(NH):
                nc.vector.tensor_scalar(b_half[:, :, h], b_sum[:, :], 1.0 / NH, None, ALU.mult).then_inc(constant_step, 1)
            dve.wait_ge(constant_step, 6)
            nc.vector.tensor_scalar(w_mean[:, :, :], w_mean[:, :, :], 1.0 / N, None, ALU.mult).then_inc(constants_ready, 1)
            nc.vector.tensor_tensor(b_centred[:, :, :], b_rows[:, :, :], b_half[:, :, :], ALU.subtract).then_inc(constants_ready, 1)
            dve.wait_ge(constants_ready, 5)
            nc.vector.tensor_scalar(b_centred[:, QUERY, :], b_centred[:, QUERY, :], INV_SQRT, None, ALU.mult).then_inc(constants_ready, 1)
            dve.wait_ge(constants_ready, CONSTANTS)

            def step(i, s):
                u, c, d = s + SPAN, s - 1, s - 2
                here = slice(s % SPAN * GROUP, (s % SPAN + 1) * GROUP)

                def centre(which, psum, ready, place, copied):
                    wait(dve, ready, count(i, s))
                    shift = offset[:, which, :, here].unsqueeze(3).broadcast_to([128, NH, GROUP, FH])
                    nc.vector.tensor_tensor(
                        place[:, s % 2, :, :].rearrange("p b (h f) -> p h b f", h=NH),
                        psum[:, :].rearrange("p (h b f) -> p h b f", h=NH, b=GROUP), shift, ALU.add,
                    ).then_inc(copied, 1)

                def values(half):
                    wait(dve, vu_ready, count(i, u, 2) - 1 + half)
                    nc.vector.tensor_tensor(
                        vu[:, u % V_RING, 2 * half:2 * half + 2, :, :].rearrange("p b g v -> p (b g) v"),
                        vu_bank[:, 0:2 * NH * VU].rearrange("p (n v) -> p n v", v=VU),
                        bvu[:, :].unsqueeze(1).broadcast_to([N, 2 * NH, VU]), ALU.add).then_inc(vu_copied, 1)

                def inverse(g):
                    wait(dve, exp_done, count(i, c, 2) - 1 + g)
                    nc.vector.reciprocal(row_inv[:, c % 2, g, :], row_sum[:, c % 2, g, :]).then_inc(inv_ready, 1)

                first_of_span = s % SPAN == 0 and exists(i, s)
                if first_of_span:
                    wait(dve, mean_ready, spans(i, s))
                    nc.vector.tensor_tensor(
                        offset[:, :, :, :], b_centred[:, :, :].unsqueeze(3).broadcast_to([128, 2, NH, SPAN_BS]),
                        misc_bank[:, 0:2 * SPAN_BS].rearrange("p (w b) -> p w b", w=2).unsqueeze(2).broadcast_to(
                            [128, 2, NH, SPAN_BS]), ALU.subtract).then_inc(offset_ready, 1)
                if exists(i, s):
                    wait(dve, offset_ready, spans(i, s))
                    centre(QUERY, q_bank, q_ready, qs, q_copied)
                if exists(i, u):
                    wait(dve, xt_copied, count(i, u))
                    nc.vector.tensor_reduce(xsum[:, :, here].rearrange("p g b -> p b g"),
                                            xt[:, u % XT_RING, :, :].rearrange("p b (g f) -> p b g f", g=NH),
                                            AX.X, ALU.add).then_inc(xsum_ready, 1)
                if exists(i, c):
                    wait(dve, s_ready, count(i, c))
                    for g in range(NH):
                        nc.vector.tensor_reduce(neg_max[:, c % 2, g, :],
                                                s_bank[g][:, :].rearrange("p (b n) -> p b n", b=GROUP),
                                                AX.X, ALU.max, negate=True).then_inc(max_ready, 1)
                if exists(i, s):
                    centre(KEY, k_bank, k_ready, ks, k_copied)
                if s % SPAN == 1 and exists(i, c):
                    wait(dve, unary_turned, spans(i, c))
                    nc.vector.tensor_copy(unary[:, c // SPAN % 2, :, :],
                                          misc_bank[:, 0:NH * SPAN_BS].rearrange("p (g b) -> p g b", g=NH)
                                          ).then_inc(unary_copied, 1)
                if first_of_span:
                    wait(dve, u_turned, spans(i, s))
                    nc.vector.tensor_reduce(
                        u_neg_max[:, :],
                        misc_bank[0:SPAN_BS, 0:NH * N].rearrange("p (g h f) -> p h g f", g=NH, h=NH),
                        AX.XY, ALU.max, negate=True).then_inc(u_max_ready, 1)
                if exists(i, u):
                    values(0)
                if exists(i, c):
                    inverse(0)
                if exists(i, u):
                    values(1)
                if exists(i, c):
                    inverse(1)
                if exists(i, d):
                    wait(dve, o_ready, count(i, d))
                    wait(dve, out_stored[d % 2], uses(i, d - 2, 2, 16))
                    nc.vector.tensor_tensor(o_sb[:, d % 2, :, :], o_bank[:, :].rearrange("p (b a) -> p b a", b=GROUP),
                                            br[:, :].unsqueeze(1).broadcast_to([F, GROUP, A]), ALU.add,
                                            ).then_inc(o_copied, 1)
                if first_of_span:
                    wait(dve, u_exp_done, spans(i, s, 2))
                    nc.vector.reciprocal(u_inv[:, :], u_sum[:, :]).then_inc(u_inv_ready, 1)
                    wait(dve, u_inv_ready, spans(i, s))
                    nc.vector.tensor_tensor(
                        u_soft[:, :, :, :], u_exp[:, :, :, :],
                        u_inv[:, :].unsqueeze(1).unsqueeze(3).broadcast_to([SPAN_BS, NH, NH, FH]), ALU.mult,
                    ).then_inc(u_soft_ready, 1)

            steps(dve, step, -SPAN, GROUPS + 2)

        @block.tensor
        def _(pe):
            soft_count = pe.alloc_register("soft_count")
            pe.reg_mov(soft_count, spans(1, 0))
            pe.wait_ge(ident_ready, 1)
            pe.wait_ge(weights_loaded, 16 * WEIGHT_DMAS)
            for n in range(4):
                last = nc.tensor.transpose(misc_bank[:, n * A:(n + 1) * A], w_rows[:, n, :], ident[:, :])
            last.then_inc(weights_turned, 1)
            nc.tensor.transpose(vu_bank[:, 0:NH], wu_rows[:, :], ident[0:NH, 0:NH]).then_inc(weights_turned, 1)
            pe.wait_ge(constants_ready, CONSTANTS)

            def step(i, s):
                u, d, c = s + SPAN, s - 2, s - 1
                j = s % SPAN

                def half_rows(g):
                    return slice(g * DPH, (g + 1) * DPH)

                def means():
                    wait(pe, xsum_ready, count(i, s + SPAN - 1))
                    wait(pe, xt_copied, count(i, s + SPAN - 1))
                    for which in (QUERY, KEY):
                        for g in range(NH):
                            last = nc.tensor.matmul(
                                misc_bank[half_rows(g), which * SPAN_BS:(which + 1) * SPAN_BS], w_mean[:, which, :],
                                xsum[:, g, :], start=True, stop=True)
                    last.then_inc(mean_ready, 1)

                def project(which, psum, ready):
                    for h in range(NH):
                        for g in range(NH):
                            last = nc.tensor.matmul(
                                psum[half_rows(g), h * GROUP * FH:(h + 1) * GROUP * FH].rearrange(
                                    "p (b f) -> p b f", b=GROUP),
                                wqk[:, which, h * DPH:(h + 1) * DPH],
                                xt[:, s % XT_RING, :, g * FH:(g + 1) * FH], start=True, stop=True)
                    last.then_inc(ready, 1)

                def turn_x():
                    wait(pe, x_loaded[u % X_RING], uses(i, u, X_RING, 16))
                    wait(pe, xt_copied, count(i, u - 1))
                    if j == 0 and exists(i, s):
                        wait(pe, offset_ready, spans(i, s))
                    if j == 1 and exists(i, s):
                        wait(pe, u_exp_done, spans(i, s, 2))
                    if j == 2 and exists(i, s):
                        wait(pe, unary_copied, spans(i, s))
                    for b in range(GROUP):
                        last = nc.tensor.transpose(misc_bank[:, b * F:(b + 1) * F], x_in[:, u % X_RING, b, :], ident[:, :])
                    last.then_inc(xt_ready, 1)

                def scores():
                    wait(pe, q_copied, count(i, c))
                    wait(pe, k_copied, count(i, c))
                    wait(pe, exp_done, count(i, c - 1, 2))
                    for b in range(GROUP):
                        for g in range(NH):
                            last = nc.tensor.matmul(s_bank[g][:, b * N:(b + 1) * N], qs[half_rows(g), c % 2, b, :],
                                                    ks[half_rows(g), c % 2, b, :], start=True, stop=True)
                    last.then_inc(s_ready, 1)

                def turn_attn(half):
                    wait(pe, attn_t_copied, count(i, d, 2) - 2 + half)
                    for b in range(2):
                        for g in range(NH):
                            at = (b * NH + g) * N
                            last = nc.tensor.transpose(t_bank[:, at:at + N], attn[:, d % 2, g, 2 * half + b, :], ident[:, :])
                    last.then_inc(attn_t_ready, 1)

                def values(half):
                    wait(pe, vu_copied, count(i, u, 2) - 2 + half)
                    for b in range(2):
                        for g in range(NH):
                            at = (b * NH + g) * VU
                            for h in range(NH):
                                last = nc.tensor.matmul(
                                    vu_bank[h * FH:(h + 1) * FH, at:at + VU],
                                    xt[:, u % XT_RING, 2 * half + b, g * FH:(g + 1) * FH], wvu[:, h, :],
                                    start=True, stop=True)
                    last.then_inc(vu_ready, 1)

                def residual():
                    wait(pe, o_copied, count(i, d - 1))
                    for b in range(GROUP):
                        nc.tensor.matmul(o_bank[:, b * A:(b + 1) * A], xt[:, d % XT_RING, b, :], wr[:, :],
                                         start=(b == 0), stop=False, skip_group_check=True)

                def weighted(half):
                    wait(pe, attn_t_copied, count(i, d, 2) - 1 + half)
                    for b in range(2 * half, 2 * half + 2):
                        for h in range(NH):
                            for g in range(NH):
                                last = nc.tensor.matmul(
                                    o_bank[g * FH:(g + 1) * FH, b * A + h * DPH:b * A + (h + 1) * DPH],
                                    attn_t[:, d % 2, b, g, h * FH:(h + 1) * FH], vu[:, d % V_RING, b, g, 0:DPH],
                                    start=False, stop=True, skip_group_check=True)
                    if half:
                        last.then_inc(o_ready, 1)

                if j == 0 and exists(i, s):
                    means()
                if exists(i, s):
                    wait(pe, q_copied, count(i, c))
                    project(QUERY, q_bank, q_ready)
                if exists(i, u):
                    turn_x()
                if exists(i, c):
                    scores()
                if exists(i, s):
                    wait(pe, k_copied, count(i, c))
                    project(KEY, k_bank, k_ready)
                if exists(i, d):
                    wait(pe, attn_ready, count(i, d, 2))
                    turn_attn(0)
                if j == 0 and exists(i, s):
                    wait(pe, vu_copied, count(i, s + SPAN - 1, 2))
                    wait(pe, xt_copied, count(i, u) if exists(i, u) else GROUPS)
                    wait(pe, offset_ready, spans(i, s))
                    ring = s % V_RING
                    for g in range(NH):
                        last = nc.tensor.transpose(
                            misc_bank[0:SPAN_BS, g * N:(g + 1) * N],
                            vu[:, ring:ring + SPAN, :, g, DPH].rearrange("p r b -> p (r b)"), ident[:, :])
                    last.then_inc(u_turned, 1)
                if j == 1 and exists(i, s):
                    wait(pe, xt_copied, count(i, u) if exists(i, u) else GROUPS)
                    wait_and_step(pe, u_soft_ready, spans(i, s), soft_count, isinstance(i, int))
                    for g in range(NH):
                        last = nc.tensor.transpose(
                            misc_bank[:, g * SPAN_BS:(g + 1) * SPAN_BS],
                            u_soft[:, g, :, :].rearrange("p h f -> p (h f)"), ident[0:SPAN_BS, 0:SPAN_BS])
                    last.then_inc(unary_turned, 1)
                if exists(i, u):
                    wait(pe, xt_copied, count(i, u))
                    values(0)
                if exists(i, d):
                    residual()
                    turn_attn(1)
                    weighted(0)
                if exists(i, u):
                    values(1)
                if exists(i, d):
                    weighted(1)

            steps(pe, step, -SPAN, GROUPS + 2)


_INS = ['r_inputs', 'L0_rec_unary_w', 'L0_rec_unary_b', 'L0_rec_wq_w', 'L0_rec_wq_b', 'L0_rec_wk_w',
        'L0_rec_wk_b', 'L0_rec_wv_w', 'L0_rec_wv_b', 'L0_rec_res_w', 'L0_rec_res_b']


def kernel(**inputs):
    import numpy as _np
    import concourse.bacc as _bacc
    from concourse import mybir as _mybir
    from concourse.bass_utils import run_bass_kernel_spmd as _run

    nc = _bacc.Bacc("TRN2", target_bir_lowering=False, num_devices=1)
    arrays, args = {}, []
    for name in _INS:
        a = _np.ascontiguousarray(inputs[name])
        arrays[f"in_{name}_dram"] = a
        args.append(nc.dram_tensor(f"in_{name}_dram", a.shape, _mybir.dt.from_np(a.dtype), kind="ExternalInput").ap())
    shape = arrays["in_r_inputs_dram"].shape
    args.append(nc.dram_tensor("out_0_dram", shape, _mybir.dt.float32, kind="ExternalOutput").ap())
    attention_kernel(nc, *args)
    r = _run(nc, [arrays], core_ids=[0])
    return r.results[0]["out_0_dram"]
```

```python
from contextlib import ExitStack

import concourse.bass as bass
from concourse import mybir

F32 = mybir.dt.float32
F32R = mybir.dt.float32r
ALU = mybir.AluOpType
ACT = mybir.ActivationFunctionType
AX = mybir.AxisListType

GROUP = 4
SPAN = 4
UNROLL = 8
QUERY, KEY = 0, 1


def attention_kernel(nc, x, unary_w, unary_b, wq_w, wq_b, wk_w, wk_b, wv_w, wv_b, res_w, res_b, out):
    BS, F, E = x.shape
    A = wq_w.shape[0]
    NH = unary_w.shape[0]
    DPH = A // NH
    FH = F // NH
    N = NH * FH
    assert NH == 2 and F == E == A == N == 128
    GROUPS = BS // GROUP
    SPAN_BS = SPAN * GROUP
    VU = A + NH
    INV_SQRT = float(DPH) ** -0.5
    LAST = GROUPS // UNROLL - 1
    assert GROUPS % UNROLL == 0 and INV_SQRT == 0.125

    def exists(i, g):
        return not isinstance(i, int) or 0 <= UNROLL * i + g < GROUPS

    def count(i, g, each=1):
        return i * (UNROLL * each) + (g + 1) * each

    def spans(i, g, each=1):
        return i * (UNROLL // SPAN * each) + (g // SPAN + 1) * each

    def uses(i, g, ring, each=1):
        return i * (UNROLL // ring * each) + (g // ring + 1) * each

    def wait(eng, sem, value):
        if not isinstance(value, int) or value > 0:
            eng.wait_ge(sem, value)

    def wait_and_step(eng, sem, value, register, peeled):
        if peeled:
            eng.wait_ge(sem, value)
        else:
            eng.wait_ge(sem, register)
            eng.reg_add(register, register, 1)

    def steps(eng, step, first, last):
        for t in range(first, UNROLL):
            step(t // UNROLL, t % UNROLL)
        with eng.Fori(1, LAST) as i:
            for s in range(UNROLL):
                step(i, s)
        for t in range(UNROLL * LAST, last):
            step(t // UNROLL, t % UNROLL)

    x_groups = x.rearrange("(t b) f e -> t f b e", b=GROUP)
    out_groups = out.rearrange("(t b) f a -> t f b a", b=GROUP)

    with ExitStack() as ctx:
        def sb(name, shape, dtype=F32):
            return ctx.enter_context(nc.sbuf_tensor(name, shape, dtype))

        BANK = 512

        def bank(name, banks=1):
            return ctx.enter_context(nc.psum_tensor(name, [128, banks * BANK], F32))

        def sem(name):
            return ctx.enter_context(nc.semaphore(name))

        X_RING, XT_RING, V_RING = 4, UNROLL, UNROLL

        ident = sb("ident", [128, 128])
        w_rows = sb("w_rows", [A, 4, E])
        wu_rows = sb("wu_rows", [NH, E])
        wqk = sb("wqk", [E, 2, A])
        wvu = sb("wvu", [E, VU])
        wr = sb("wr", [E, A])
        wqk_hi = sb("wqk_hi", [E, 2, A], F32R)
        wqk_lo = sb("wqk_lo", [E, 2, A], F32R)
        w_mean = sb("w_mean", [E, 2, NH, DPH])
        b_own = sb("b_own", [A, 2])
        b_other = sb("b_other", [A, 2])
        b_centred = sb("b_centred", [A, 2])
        bvu = sb("bvu", [F, VU])
        br = sb("br", [128, A])

        x_in = sb("x_in", [F, X_RING, GROUP, E])
        xt = sb("xt", [E, XT_RING, GROUP, F])
        xt_hi = sb("xt_hi", [E, XT_RING, GROUP, F], F32R)
        xt_lo = sb("xt_lo", [E, XT_RING, GROUP, F], F32R)
        xsum = sb("xsum", [E, NH, SPAN_BS])
        offset = sb("offset", [A, 2, NH, SPAN_BS])
        v = sb("v", [N, V_RING, GROUP, NH, DPH])
        u_logit = sb("u_logit", [F, SPAN_BS, NH])
        qs = sb("qs", [128, 2, GROUP, N])
        ks = sb("ks", [128, 2, GROUP, N])
        neg_max = sb("neg_max", [N, 2, NH, GROUP])
        row_sum = sb("row_sum", [N, 2, NH, GROUP])
        row_inv = sb("row_inv", [N, 2, NH, GROUP])
        attn = sb("attn", [N, 2, NH, GROUP, N])
        attn_t = sb("attn_t", [N, 2, GROUP, NH, N])
        o_sb = sb("o_sb", [F, 2, GROUP, A])
        u_neg_max = sb("u_neg_max", [SPAN_BS, NH])
        u_exp = sb("u_exp", [SPAN_BS, NH, F])
        u_sum = sb("u_sum", [SPAN_BS, NH])
        u_inv = sb("u_inv", [SPAN_BS, NH])
        u_soft = sb("u_soft", [SPAN_BS, NH, NH, FH])
        unary = sb("unary", [N, 2, NH, SPAN_BS])

        vu_banks = bank("vu_banks", 2)
        misc_bank = bank("misc_bank")
        qk_bank = bank("qk_bank")
        s_bank = [bank("s_bank0"), bank("s_bank1")]
        t_bank = bank("t_bank")
        o_bank = bank("o_bank")

        x_loaded = [sem(f"x_loaded{r}") for r in range(X_RING)]
        out_stored = [sem(f"out_stored{r}") for r in range(2)]
        weights_loaded = sem("weights_loaded")
        ident_zeroed = sem("ident_zeroed")
        ident_ready = sem("ident_ready")
        weights_turned = sem("weights_turned")
        constant_step = sem("constant_step")
        constants_ready = sem("constants_ready")
        xt_ready, xt_copied = sem("xt_ready"), sem("xt_copied")
        xt_hi_ready, xt_split = sem("xt_hi_ready"), sem("xt_split")
        xsum_ready = sem("xsum_ready")
        mean_ready, offset_ready = sem("mean_ready"), sem("offset_ready")
        vu_ready, vu_copied = sem("vu_ready"), sem("vu_copied")
        q_ready, q_copied = sem("q_ready"), sem("q_copied")
        k_ready, k_copied = sem("k_ready"), sem("k_copied")
        s_ready = sem("s_ready")
        max_ready = sem("max_ready")
        exp_done = sem("exp_done")
        inv_ready = sem("inv_ready")
        attn_ready = sem("attn_ready")
        attn_t_ready, attn_t_copied = sem("attn_t_ready"), sem("attn_t_copied")
        o_ready, o_copied = sem("o_ready"), sem("o_copied")
        out_ready = sem("out_ready")
        u_turned = sem("u_turned")
        u_max_ready = sem("u_max_ready")
        u_exp_done = sem("u_exp_done")
        u_inv_ready = sem("u_inv_ready")
        u_soft_ready = sem("u_soft_ready")
        unary_turned, unary_copied = sem("unary_turned"), sem("unary_copied")

        WEIGHT_DMAS = 5 + 8 + 3
        CONSTANTS = 8

        block = ctx.enter_context(nc.Block())

        @block.sync
        def _(sp):
            for n, w in enumerate((wq_w, wk_w, wv_w, res_w)):
                sp.dma_start(w_rows[:, n, :], w).then_inc(weights_loaded, 16)
            sp.dma_start(wu_rows[:, :], unary_w).then_inc(weights_loaded, 16)
            for half in range(2):
                here = slice(half * DPH, (half + 1) * DPH)
                other = slice((1 - half) * DPH, (2 - half) * DPH)
                for which, bias in ((QUERY, wq_b), (KEY, wk_b)):
                    sp.dma_start(b_own[here, which:which + 1], bias[here].unsqueeze(1)).then_inc(weights_loaded, 16)
                    sp.dma_start(b_other[here, which:which + 1], bias[other].unsqueeze(1)).then_inc(weights_loaded, 16)
            sp.dma_start(bvu[:, 0:A], wv_b.partition_broadcast(F)).then_inc(weights_loaded, 16)
            sp.dma_start(bvu[:, A:VU], unary_b.partition_broadcast(F)).then_inc(weights_loaded, 16)
            sp.dma_start(br[:, :], res_b.partition_broadcast(F)).then_inc(weights_loaded, 16)

            def step(i, s):
                ahead = s + 2 * SPAN
                if exists(i, ahead):
                    wait(sp, xt_ready, count(i, ahead - X_RING))
                    sp.dma_start(x_in[:, ahead % X_RING, :, :], x_groups[UNROLL * i + ahead]).then_inc(
                        x_loaded[ahead % X_RING], 16)
                if exists(i, s - 3):
                    wait(sp, out_ready, count(i, s - 3))
                    sp.dma_start(out_groups[UNROLL * i + (s - 3)], o_sb[:, (s - 3) % 2, :, :]).then_inc(
                        out_stored[(s - 3) % 2], 16)

            steps(sp, step, -2 * SPAN, GROUPS + 3)
            for r in range(2):
                sp.wait_ge(out_stored[r], 16 * (GROUPS // 2))

        @block.gpsimd
        def _(pool):
            inv_count, unary_count = pool.alloc_register("inv_count"), pool.alloc_register("unary_count")
            pool.reg_mov(inv_count, count(1, -1, 2) - 1)
            pool.reg_mov(unary_count, spans(1, 0))
            nc.gpsimd.memset(ident[:, :], 0.0).then_inc(ident_zeroed, 1)
            pool.wait_ge(ident_zeroed, 1)
            nc.gpsimd.affine_select(out=ident[:, :], in_=ident[:, :], compare_op=ALU.not_equal, fill=1.0,
                                    base=0, pattern=[[-1, 128]], channel_multiplier=1).then_inc(ident_ready, 1)

            def step(i, s):
                c, e = s - 1, s - 3
                if exists(i, e):
                    wait(pool, o_copied, count(i, e))
                    nc.gpsimd.tensor_tensor(o_sb[:, e % 2, :, :], o_sb[:, e % 2, :, :],
                                            br[:, :].unsqueeze(1).broadcast_to([F, GROUP, A]), ALU.add,
                                            ).then_inc(out_ready, 1)
                if not exists(i, c):
                    return
                if c % SPAN == 0:
                    wait_and_step(pool, unary_copied, spans(i, c), unary_count, isinstance(i, int))
                for g in range(NH):
                    wait_and_step(pool, inv_ready, count(i, c, 2) - 1 + g, inv_count, isinstance(i, int))
                    for b in range(GROUP):
                        at = (c % SPAN) * GROUP + b
                        last = nc.gpsimd.tensor_scalar(
                            attn[:, c % 2, g, b, :], attn[:, c % 2, g, b, :], row_inv[:, c % 2, g, b:b + 1],
                            unary[:, c // SPAN % 2, g, at:at + 1], ALU.mult, ALU.add)
                    last.then_inc(attn_ready, 1)

            steps(pool, step, 0, GROUPS + 3)

        @block.scalar
        def _(act):
            def step(i, s):
                u, c, d, e = s + SPAN, s - 1, s - 2, s - 3

                def attn_t_copy(half):
                    wait(act, attn_t_ready, count(i, d, 2) - 1 + half)
                    nc.scalar.copy(attn_t[:, d % 2, 2 * half:2 * half + 2, :, :].rearrange("p b g n -> p (b g n)"),
                                   t_bank[:, :]).then_inc(attn_t_copied, 1)

                def exponentials(g, batch):
                    for b in batch:
                        last = nc.scalar.activation(
                            attn[:, c % 2, g, b, :], s_bank[g][:, b * N:(b + 1) * N], ACT.Exp,
                            bias=neg_max[:, c % 2, g, b:b + 1], scale=1.0,
                            accum_out=row_sum[:, c % 2, g, b:b + 1])
                    if batch[-1] == GROUP - 1:
                        last.then_inc(exp_done, 1)

                if exists(i, e):
                    wait(act, o_ready, count(i, e))
                    wait(act, out_stored[e % 2], uses(i, e - 2, 2, 16))
                    nc.scalar.copy(o_sb[:, e % 2, :, :].rearrange("p b a -> p (b a)"), o_bank[:, :]).then_inc(o_copied, 1)
                if exists(i, u):
                    wait(act, xt_ready, count(i, u))
                    nc.scalar.copy(xt[:, u % XT_RING, :, :].rearrange("p b f -> p (b f)"),
                                   misc_bank[:, :]).then_inc(xt_copied, 1)
                    nc.scalar.copy(xt_hi[:, u % XT_RING, :, :].rearrange("p b f -> p (b f)"),
                                   misc_bank[:, :]).then_inc(xt_hi_ready, 1)
                if exists(i, d):
                    attn_t_copy(0)
                if exists(i, c):
                    wait(act, max_ready, count(i, c, 2) - 1)
                    exponentials(0, range(0, 4))
                if exists(i, d):
                    attn_t_copy(1)
                if exists(i, c):
                    wait(act, max_ready, count(i, c, 2))
                    exponentials(1, range(0, 4))
                if s % SPAN == 0 and exists(i, s):
                    wait(act, u_max_ready, spans(i, s))
                    for h in range(NH):
                        nc.scalar.activation(u_exp[:, h, :], misc_bank[0:SPAN_BS, h * F:(h + 1) * F], ACT.Exp,
                                             bias=u_neg_max[:, h:h + 1], scale=1.0,
                                             accum_out=u_sum[:, h:h + 1]).then_inc(u_exp_done, 1)

            steps(act, step, -SPAN, GROUPS + 3)

        @block.vector
        def _(dve):
            dve.wait_ge(weights_loaded, 16 * WEIGHT_DMAS)
            dve.wait_ge(weights_turned, 2)
            wt = misc_bank[:, :].rearrange("p (w a) -> p w a", w=4)
            nc.vector.tensor_scalar(wqk[:, QUERY, :], wt[:, 0, :], INV_SQRT, None, ALU.mult).then_inc(constant_step, 1)
            nc.vector.tensor_copy(wqk[:, KEY, :], wt[:, 1, :]).then_inc(constant_step, 1)
            nc.vector.tensor_copy(wvu[:, 0:A], wt[:, 2, :]).then_inc(constants_ready, 1)
            nc.vector.tensor_copy(wr[:, :], wt[:, 3, :]).then_inc(constants_ready, 1)
            nc.vector.tensor_copy(wvu[:, A:VU], vu_banks[:, 0:NH]).then_inc(constants_ready, 1)
            nc.vector.tensor_tensor(b_centred[:, :], b_own[:, :], b_other[:, :], ALU.subtract).then_inc(constant_step, 1)
            dve.wait_ge(constant_step, 3)
            nc.vector.tensor_scalar(b_centred[:, QUERY:KEY], b_centred[:, QUERY:KEY], INV_SQRT / NH, None,
                                    ALU.mult).then_inc(constants_ready, 1)
            nc.vector.tensor_scalar(b_centred[:, KEY:], b_centred[:, KEY:], 1.0 / NH, None, ALU.mult).then_inc(constants_ready, 1)
            nc.vector.tensor_copy(wqk_hi[:, :, :], wqk[:, :, :]).then_inc(constant_step, 1)
            for r in range(2):
                nc.vector.tensor_tensor(w_mean[:, :, r, :], wqk[:, :, 0:DPH], wqk[:, :, DPH:A], ALU.add).then_inc(constant_step, 1)
            dve.wait_ge(constant_step, 6)
            nc.vector.tensor_tensor(wqk_lo[:, :, :], wqk[:, :, :], wqk_hi[:, :, :].bitcast(F32), ALU.subtract).then_inc(constants_ready, 1)
            for r in range(2):
                nc.vector.tensor_scalar(w_mean[:, :, r, :], w_mean[:, :, r, :], 1.0 / N, None, ALU.mult).then_inc(constants_ready, 1)
            dve.wait_ge(constants_ready, CONSTANTS)

            def step(i, s):
                u, c = s + SPAN, s - 1
                here = slice(s % SPAN * GROUP, (s % SPAN + 1) * GROUP)

                def centre(which, psum, ready, place, copied):
                    wait(dve, ready, count(i, s))
                    by_g = psum[:, :].rearrange("p (b g f) -> p b g f", b=GROUP, g=NH)
                    for h in range(NH):
                        rows = slice(h * DPH, (h + 1) * DPH)
                        for g in range(NH):
                            last = nc.vector.tensor_tensor(
                                place[g * DPH:(g + 1) * DPH, s % 2, :, h * FH:(h + 1) * FH], by_g[rows, :, g, :],
                                offset[rows, which, g, here].unsqueeze(2).broadcast_to([DPH, GROUP, FH]), ALU.add)
                    last.then_inc(copied, 1)

                def values():
                    wait(dve, vu_ready, count(i, u))
                    by_bank = vu_banks[:, :].rearrange("p (k n) -> p k n", k=2)[:, :, 0:2 * VU].rearrange(
                        "p k (b v) -> p k b v", b=2)
                    nc.vector.tensor_tensor(
                        u_logit[:, here, :].rearrange("p (k b) h -> p k b h", k=2), by_bank[:, :, :, A:VU],
                        bvu[:, A:VU].unsqueeze(1).unsqueeze(1).broadcast_to([F, 2, 2, NH]), ALU.add)
                    for g in range(NH):
                        rows = slice(g * FH, (g + 1) * FH)
                        for h in range(NH):
                            cols = slice(h * DPH, (h + 1) * DPH)
                            last = nc.vector.tensor_tensor(
                                v[h * FH:(h + 1) * FH, u % V_RING, :, g, :].rearrange("p (k b) d -> p k b d", k=2),
                                by_bank[rows, :, :, cols],
                                bvu[rows, cols].unsqueeze(1).unsqueeze(1).broadcast_to([FH, 2, 2, DPH]), ALU.add)
                    last.then_inc(vu_copied, 1)

                def inverse(g):
                    wait(dve, exp_done, count(i, c, 2) - 1 + g)
                    nc.vector.reciprocal(row_inv[:, c % 2, g, :], row_sum[:, c % 2, g, :]).then_inc(inv_ready, 1)

                first_of_span = s % SPAN == 0 and exists(i, s)
                if first_of_span:
                    wait(dve, mean_ready, spans(i, s))
                    wait(dve, k_copied, count(i, s - 1))
                    nc.vector.tensor_tensor(
                        offset[:, :, :, :].rearrange("p w g b -> p w (g b)"),
                        b_centred[:, :].unsqueeze(2).broadcast_to([A, 2, NH * SPAN_BS]),
                        misc_bank[:, 0:2 * NH * SPAN_BS].rearrange("p (w n) -> p w n", w=2),
                        ALU.subtract).then_inc(offset_ready, 1)
                if exists(i, s):
                    wait(dve, offset_ready, spans(i, s))
                    centre(QUERY, qk_bank, q_ready, qs, q_copied)
                if exists(i, u):
                    wait(dve, xt_copied, count(i, u))
                    nc.vector.tensor_reduce(xsum[:, :, here].rearrange("p g b -> p b g"),
                                            xt[:, u % XT_RING, :, :].rearrange("p b (g f) -> p b g f", g=NH),
                                            AX.X, ALU.add).then_inc(xsum_ready, 1)
                    wait(dve, xt_hi_ready, count(i, u))
                    nc.vector.tensor_tensor(xt_lo[:, u % XT_RING, :, :].rearrange("p b f -> p (b f)"), misc_bank[:, :],
                                            xt_hi[:, u % XT_RING, :, :].rearrange("p b f -> p (b f)").bitcast(F32),
                                            ALU.subtract).then_inc(xt_split, 1)
                if exists(i, c):
                    wait(dve, s_ready, count(i, c))
                    for g in range(NH):
                        nc.vector.tensor_reduce(neg_max[:, c % 2, g, :],
                                                s_bank[g][:, :].rearrange("p (b n) -> p b n", b=GROUP),
                                                AX.X, ALU.max, negate=True).then_inc(max_ready, 1)
                if exists(i, s):
                    centre(KEY, qk_bank, k_ready, ks, k_copied)
                if s % SPAN == 1 and exists(i, c):
                    wait(dve, unary_turned, spans(i, c))
                    nc.vector.tensor_copy(unary[:, c // SPAN % 2, :, :],
                                          misc_bank[:, 0:NH * SPAN_BS].rearrange("p (g b) -> p g b", g=NH)
                                          ).then_inc(unary_copied, 1)
                if first_of_span:
                    wait(dve, u_turned, spans(i, s))
                    nc.vector.tensor_reduce(
                        u_neg_max[:, :],
                        misc_bank[0:SPAN_BS, 0:NH * F].rearrange("p (h n) -> p h n", h=NH),
                        AX.X, ALU.max, negate=True).then_inc(u_max_ready, 1)
                if exists(i, u):
                    values()
                if exists(i, c):
                    inverse(0)
                    inverse(1)
                if first_of_span:
                    wait(dve, u_exp_done, spans(i, s, 2))
                    nc.vector.reciprocal(u_inv[:, :], u_sum[:, :]).then_inc(u_inv_ready, 1)
                    wait(dve, u_inv_ready, spans(i, s))
                    nc.vector.tensor_tensor(
                        u_soft[:, :, :, :].rearrange("p g h f -> p h g f"),
                        u_exp[:, :, :].rearrange("p h (g f) -> p h g f", g=NH),
                        u_inv[:, :].unsqueeze(2).unsqueeze(3).broadcast_to([SPAN_BS, NH, NH, FH]), ALU.mult,
                    ).then_inc(u_soft_ready, 1)

            steps(dve, step, -SPAN, GROUPS + 1)

        @block.tensor
        def _(pe):
            soft_count = pe.alloc_register("soft_count")
            pe.reg_mov(soft_count, spans(1, 0))
            pe.wait_ge(ident_ready, 1)
            pe.wait_ge(weights_loaded, 16 * WEIGHT_DMAS)
            for n in range(4):
                last = nc.tensor.transpose(misc_bank[:, n * A:(n + 1) * A], w_rows[:, n, :], ident[:, :])
            last.then_inc(weights_turned, 1)
            nc.tensor.transpose(vu_banks[:, 0:NH], wu_rows[:, :], ident[0:NH, 0:NH]).then_inc(weights_turned, 1)
            pe.wait_ge(constants_ready, CONSTANTS)

            def step(i, s):
                u, d, c = s + SPAN, s - 2, s - 1
                j = s % SPAN

                def half_rows(g):
                    return slice(g * DPH, (g + 1) * DPH)

                def means():
                    wait(pe, xsum_ready, count(i, s + SPAN - 1))
                    wait(pe, xt_split, count(i, s + SPAN - 1))
                    for which in (QUERY, KEY):
                        last = nc.tensor.matmul(
                            misc_bank[:, which * NH * SPAN_BS:(which + 1) * NH * SPAN_BS],
                            w_mean[:, which, :, :].rearrange("p r d -> p (r d)"),
                            xsum[:, :, :].rearrange("p g b -> p (g b)"), start=True, stop=True)
                    last.then_inc(mean_ready, 1)

                def project(which, psum, ready):
                    hi, lo = (x[:, s % XT_RING, :, :].rearrange("p b f -> p (b f)") for x in (xt_hi, xt_lo))
                    nc.tensor.matmul(psum[:, :], wqk_lo[:, which, :], hi, start=True, stop=False)
                    nc.tensor.matmul(psum[:, :], wqk_hi[:, which, :], lo, start=False, stop=False)
                    nc.tensor.matmul(psum[:, :], wqk_hi[:, which, :], hi, start=False, stop=True).then_inc(ready, 1)

                def turn_x():
                    wait(pe, x_loaded[u % X_RING], uses(i, u, X_RING, 16))
                    wait(pe, xt_split, count(i, u - 1))
                    if j == 0 and exists(i, s):
                        wait(pe, offset_ready, spans(i, s))
                    if j == 1 and exists(i, s):
                        wait(pe, u_exp_done, spans(i, s, 2))
                    if j == 2 and exists(i, s):
                        wait(pe, unary_copied, spans(i, s))
                    for b in range(GROUP):
                        last = nc.tensor.transpose(misc_bank[:, b * F:(b + 1) * F], x_in[:, u % X_RING, b, :], ident[:, :])
                    last.then_inc(xt_ready, 1)

                def scores():
                    wait(pe, q_copied, count(i, c))
                    wait(pe, k_copied, count(i, c))
                    wait(pe, exp_done, count(i, c - 1, 2))
                    for b in range(GROUP):
                        for g in range(NH):
                            last = nc.tensor.matmul(s_bank[g][:, b * N:(b + 1) * N], qs[half_rows(g), c % 2, b, :],
                                                    ks[half_rows(g), c % 2, b, :], start=True, stop=True)
                    last.then_inc(s_ready, 1)

                def turn_attn(half):
                    wait(pe, attn_t_copied, count(i, d, 2) - 2 + half)
                    for b in range(2):
                        for g in range(NH):
                            at = (b * NH + g) * N
                            last = nc.tensor.transpose(t_bank[:, at:at + N], attn[:, d % 2, g, 2 * half + b, :], ident[:, :])
                    last.then_inc(attn_t_ready, 1)

                def values():
                    wait(pe, xt_copied, count(i, u))
                    wait(pe, vu_copied, count(i, u - 1))
                    for b in range(GROUP):
                        at = b // 2 * BANK + b % 2 * VU
                        last = nc.tensor.matmul(vu_banks[:, at:at + VU], xt[:, u % XT_RING, b, :], wvu[:, :],
                                                start=True, stop=True)
                    last.then_inc(vu_ready, 1)

                def residual():
                    wait(pe, o_copied, count(i, d - 1))
                    for b in range(GROUP):
                        nc.tensor.matmul(o_bank[:, b * A:(b + 1) * A], xt[:, d % XT_RING, b, :], wr[:, :],
                                         start=(b == 0), stop=False, skip_group_check=True)

                def weighted(half):
                    wait(pe, attn_t_copied, count(i, d, 2) - 1 + half)
                    for b in range(2 * half, 2 * half + 2):
                        for h in range(NH):
                            for g in range(NH):
                                last = nc.tensor.matmul(
                                    o_bank[g * FH:(g + 1) * FH, b * A + h * DPH:b * A + (h + 1) * DPH],
                                    attn_t[:, d % 2, b, g, h * FH:(h + 1) * FH], v[:, d % V_RING, b, g, :],
                                    start=False, stop=True, skip_group_check=True)
                    if half:
                        last.then_inc(o_ready, 1)

                if j == 0 and exists(i, s):
                    means()
                if exists(i, s):
                    wait(pe, k_copied, count(i, c))
                    project(QUERY, qk_bank, q_ready)
                if exists(i, u):
                    turn_x()
                if exists(i, c):
                    scores()
                if exists(i, s):
                    wait(pe, q_copied, count(i, s))
                    project(KEY, qk_bank, k_ready)
                if exists(i, d):
                    wait(pe, attn_ready, count(i, d, 2))
                    turn_attn(0)
                if j == 0 and exists(i, s):
                    wait(pe, vu_copied, count(i, s + SPAN - 1))
                    wait(pe, xt_split, count(i, u) if exists(i, u) else GROUPS)
                    wait(pe, offset_ready, spans(i, s))
                    for h in range(NH):
                        last = nc.tensor.transpose(
                            misc_bank[0:SPAN_BS, h * F:(h + 1) * F],
                            u_logit[:, :, h], ident[:, :])
                    last.then_inc(u_turned, 1)
                if j == 1 and exists(i, s):
                    wait(pe, xt_split, count(i, u) if exists(i, u) else GROUPS)
                    wait_and_step(pe, u_soft_ready, spans(i, s), soft_count, isinstance(i, int))
                    for g in range(NH):
                        last = nc.tensor.transpose(
                            misc_bank[:, g * SPAN_BS:(g + 1) * SPAN_BS],
                            u_soft[:, g, :, :].rearrange("p h f -> p (h f)"), ident[0:SPAN_BS, 0:SPAN_BS])
                    last.then_inc(unary_turned, 1)
                if exists(i, u):
                    values()
                if exists(i, d):
                    residual()
                    turn_attn(1)
                    weighted(0)
                    weighted(1)

            steps(pe, step, -SPAN, GROUPS + 2)


_INS = ['r_inputs', 'L0_rec_unary_w', 'L0_rec_unary_b', 'L0_rec_wq_w', 'L0_rec_wq_b', 'L0_rec_wk_w',
        'L0_rec_wk_b', 'L0_rec_wv_w', 'L0_rec_wv_b', 'L0_rec_res_w', 'L0_rec_res_b']


def kernel(**inputs):
    import numpy as _np
    import concourse.bacc as _bacc
    from concourse import mybir as _mybir
    from concourse.bass_utils import run_bass_kernel_spmd as _run

    nc = _bacc.Bacc("TRN2", target_bir_lowering=False, num_devices=1)
    arrays, args = {}, []
    for name in _INS:
        a = _np.ascontiguousarray(inputs[name])
        arrays[f"in_{name}_dram"] = a
        args.append(nc.dram_tensor(f"in_{name}_dram", a.shape, _mybir.dt.from_np(a.dtype), kind="ExternalInput").ap())
    shape = arrays["in_r_inputs_dram"].shape
    args.append(nc.dram_tensor("out_0_dram", shape, _mybir.dt.float32, kind="ExternalOutput").ap())
    attention_kernel(nc, *args)
    r = _run(nc, [arrays], core_ids=[0])
    return r.results[0]["out_0_dram"]
```

```python
from contextlib import ExitStack

import concourse.bass as bass
from concourse import mybir

F32 = mybir.dt.float32
F32R = mybir.dt.float32r
ALU = mybir.AluOpType
ACT = mybir.ActivationFunctionType
AX = mybir.AxisListType

GROUP = 4
SPAN = 8
UNROLL = 16
QUERY, KEY = 0, 1


def attention_kernel(nc, x, unary_w, unary_b, wq_w, wq_b, wk_w, wk_b, wv_w, wv_b, res_w, res_b, out):
    BS, F, E = x.shape
    A = wq_w.shape[0]
    NH = unary_w.shape[0]
    DPH = A // NH
    FH = F // NH
    N = NH * FH
    assert NH == 2 and F == E == A == N == 128
    GROUPS = BS // GROUP
    SPAN_BS = SPAN * GROUP
    VU = A + NH
    INV_SQRT = float(DPH) ** -0.5
    LAST = GROUPS // UNROLL - 1
    assert GROUPS % UNROLL == 0 and INV_SQRT == 0.125

    def exists(i, g):
        return not isinstance(i, int) or 0 <= UNROLL * i + g < GROUPS

    def count(i, g, each=1):
        return i * (UNROLL * each) + (g + 1) * each

    def spans(i, g, each=1):
        return i * (UNROLL // SPAN * each) + (g // SPAN + 1) * each

    def uses(i, g, ring, each=1):
        return i * (UNROLL // ring * each) + (g // ring + 1) * each

    def wait(eng, sem, value):
        if not isinstance(value, int) or value > 0:
            eng.wait_ge(sem, value)

    def wait_and_step(eng, sem, value, register, peeled):
        if peeled:
            eng.wait_ge(sem, value)
        else:
            eng.wait_ge(sem, register)
            eng.reg_add(register, register, 1)

    def steps(eng, step, first, last):
        for t in range(first, UNROLL):
            step(t // UNROLL, t % UNROLL)
        with eng.Fori(1, LAST) as i:
            for s in range(UNROLL):
                step(i, s)
        for t in range(UNROLL * LAST, last):
            step(t // UNROLL, t % UNROLL)

    x_groups = x.rearrange("(t b) f e -> t f b e", b=GROUP)
    out_groups = out.rearrange("(t b) f a -> t f b a", b=GROUP)

    with ExitStack() as ctx:
        def sb(name, shape, dtype=F32):
            return ctx.enter_context(nc.sbuf_tensor(name, shape, dtype))

        BANK = 512

        def bank(name, banks=1):
            return ctx.enter_context(nc.psum_tensor(name, [128, banks * BANK], F32))

        def sem(name):
            return ctx.enter_context(nc.semaphore(name))

        X_RING, XT_RING, V_RING, ATTN_RING = 4, UNROLL, UNROLL, 4

        ident = sb("ident", [128, 128])
        w_rows = sb("w_rows", [A, 4, E])
        wu_rows = sb("wu_rows", [NH, E])
        wqk = sb("wqk", [E, 2, A])
        wvu = sb("wvu", [E, VU])
        wr = sb("wr", [E, A])
        wqk_hi = sb("wqk_hi", [E, 2, A], F32R)
        wqk_lo = sb("wqk_lo", [E, 2, A], F32R)
        w_mean = sb("w_mean", [E, 2, NH, DPH])
        b_own = sb("b_own", [A, 2])
        b_other = sb("b_other", [A, 2])
        b_centred = sb("b_centred", [A, 2])
        bvu = sb("bvu", [F, VU])
        br = sb("br", [128, A])

        x_in = sb("x_in", [F, X_RING, GROUP, E])
        xt = sb("xt", [E, XT_RING, GROUP, F])
        xt_hi = sb("xt_hi", [E, XT_RING, GROUP, F], F32R)
        xt_lo = sb("xt_lo", [E, XT_RING, GROUP, F], F32R)
        xsum = sb("xsum", [E, NH, SPAN_BS])
        offset = sb("offset", [A, 2, NH, SPAN_BS])
        v = sb("v", [N, V_RING, GROUP, NH, DPH])
        u_logit = sb("u_logit", [F, SPAN_BS, NH])
        qs = sb("qs", [128, 2, GROUP, N])
        ks = sb("ks", [128, 2, GROUP, N])
        neg_max = sb("neg_max", [N, 2, NH, GROUP])
        row_sum = sb("row_sum", [N, 2, NH, GROUP])
        row_inv = sb("row_inv", [N, 2, NH, GROUP])
        attn = sb("attn", [N, ATTN_RING, NH, GROUP, N])
        attn_t = sb("attn_t", [N, 2, GROUP, NH, N])
        o_sb = sb("o_sb", [F, 2, GROUP, A])
        u_neg_max = sb("u_neg_max", [SPAN_BS, NH])
        u_exp = sb("u_exp", [SPAN_BS, NH, F])
        u_sum = sb("u_sum", [SPAN_BS, NH])
        u_inv = sb("u_inv", [SPAN_BS, NH])
        u_soft = sb("u_soft", [SPAN_BS, NH, NH, FH])
        unary = sb("unary", [N, 2, NH, SPAN_BS])

        vu_banks = bank("vu_banks", 2)
        misc_bank = bank("misc_bank")
        qk_bank = bank("qk_bank")
        s_bank = [bank("s_bank0"), bank("s_bank1")]
        t_bank = bank("t_bank")
        o_bank = bank("o_bank")

        x_loaded = [sem(f"x_loaded{r}") for r in range(X_RING)]
        out_stored = [sem(f"out_stored{r}") for r in range(2)]
        weights_loaded = sem("weights_loaded")
        ident_zeroed = sem("ident_zeroed")
        ident_ready = sem("ident_ready")
        weights_turned = sem("weights_turned")
        constant_step = sem("constant_step")
        constants_ready = sem("constants_ready")
        xt_ready, xt_copied = sem("xt_ready"), sem("xt_copied")
        xt_hi_ready, xt_lo_ready = sem("xt_hi_ready"), sem("xt_lo_ready")
        xsum_ready = sem("xsum_ready")
        mean_ready, offset_ready = sem("mean_ready"), sem("offset_ready")
        vu_ready, vu_copied = sem("vu_ready"), sem("vu_copied")
        q_ready, q_copied = sem("q_ready"), sem("q_copied")
        k_ready, k_copied = sem("k_ready"), sem("k_copied")
        s_ready = sem("s_ready")
        max_ready = sem("max_ready")
        exp_done = sem("exp_done")
        inv_ready = sem("inv_ready")
        attn_ready = sem("attn_ready")
        attn_t_ready, attn_t_copied = sem("attn_t_ready"), sem("attn_t_copied")
        o_ready, o_copied = sem("o_ready"), sem("o_copied")
        out_ready = sem("out_ready")
        u_turned = sem("u_turned")
        u_max_ready = sem("u_max_ready")
        u_exp_done = sem("u_exp_done")
        u_inv_ready = sem("u_inv_ready")
        u_soft_ready = sem("u_soft_ready")
        unary_turned, unary_copied = sem("unary_turned"), sem("unary_copied")

        WEIGHT_DMAS = 5 + 8 + 3
        CONSTANTS = 8

        block = ctx.enter_context(nc.Block())

        @block.sync
        def _(sp):
            for n, w in enumerate((wq_w, wk_w, wv_w, res_w)):
                sp.dma_start(w_rows[:, n, :], w).then_inc(weights_loaded, 16)
            sp.dma_start(wu_rows[:, :], unary_w).then_inc(weights_loaded, 16)
            for half in range(2):
                here = slice(half * DPH, (half + 1) * DPH)
                other = slice((1 - half) * DPH, (2 - half) * DPH)
                for which, bias in ((QUERY, wq_b), (KEY, wk_b)):
                    sp.dma_start(b_own[here, which:which + 1], bias[here].unsqueeze(1)).then_inc(weights_loaded, 16)
                    sp.dma_start(b_other[here, which:which + 1], bias[other].unsqueeze(1)).then_inc(weights_loaded, 16)
            sp.dma_start(bvu[:, 0:A], wv_b.partition_broadcast(F)).then_inc(weights_loaded, 16)
            sp.dma_start(bvu[:, A:VU], unary_b.partition_broadcast(F)).then_inc(weights_loaded, 16)
            sp.dma_start(br[:, :], res_b.partition_broadcast(F)).then_inc(weights_loaded, 16)

            def step(i, s):
                ahead = s + SPAN + X_RING
                if exists(i, ahead):
                    wait(sp, xt_ready, count(i, ahead - X_RING))
                    sp.dma_start(x_in[:, ahead % X_RING, :, :], x_groups[UNROLL * i + ahead]).then_inc(
                        x_loaded[ahead % X_RING], 16)
                e = s - 4
                if exists(i, e):
                    wait(sp, out_ready, count(i, e))
                    sp.dma_start(out_groups[UNROLL * i + e], o_sb[:, e % 2, :, :]).then_inc(out_stored[e % 2], 16)

            steps(sp, step, -SPAN - X_RING, GROUPS + 4)
            for r in range(2):
                sp.wait_ge(out_stored[r], 16 * (GROUPS // 2))

        @block.gpsimd
        def _(pool):
            inv_count, unary_count = pool.alloc_register("inv_count"), pool.alloc_register("unary_count")
            pool.reg_mov(inv_count, count(1, -1, 2) - 1)
            pool.reg_mov(unary_count, spans(1, 0))
            nc.gpsimd.memset(ident[:, :], 0.0).then_inc(ident_zeroed, 1)
            pool.wait_ge(ident_zeroed, 1)
            nc.gpsimd.affine_select(out=ident[:, :], in_=ident[:, :], compare_op=ALU.not_equal, fill=1.0,
                                    base=0, pattern=[[-1, 128]], channel_multiplier=1).then_inc(ident_ready, 1)

            def step(i, s):
                u, c, e = s + SPAN, s - 1, s - 4
                if exists(i, e):
                    wait(pool, o_copied, count(i, e))
                    nc.gpsimd.tensor_tensor(o_sb[:, e % 2, :, :], o_sb[:, e % 2, :, :],
                                            br[:, :].unsqueeze(1).broadcast_to([F, GROUP, A]), ALU.add,
                                            ).then_inc(out_ready, 1)
                if exists(i, u):
                    wait(pool, xt_hi_ready, count(i, u))
                    nc.gpsimd.tensor_tensor(xt_lo[:, u % XT_RING, :, :], xt[:, u % XT_RING, :, :],
                                            xt_hi[:, u % XT_RING, :, :].bitcast(F32), ALU.subtract,
                                            ).then_inc(xt_lo_ready, 1)
                if not exists(i, c):
                    return
                if c % SPAN == 0:
                    wait_and_step(pool, unary_copied, spans(i, c), unary_count, isinstance(i, int))
                for g in range(NH):
                    wait_and_step(pool, inv_ready, count(i, c, 2) - 1 + g, inv_count, isinstance(i, int))
                    for b in range(GROUP):
                        at = (c % SPAN) * GROUP + b
                        last = nc.gpsimd.tensor_scalar(
                            attn[:, c % ATTN_RING, g, b, :], attn[:, c % ATTN_RING, g, b, :], row_inv[:, c % 2, g, b:b + 1],
                            unary[:, c // SPAN % 2, g, at:at + 1], ALU.mult, ALU.add)
                    last.then_inc(attn_ready, 1)

            steps(pool, step, -SPAN, GROUPS + 4)

        @block.scalar
        def _(act):
            def step(i, s):
                u, c, d, e = s + SPAN, s - 1, s - 3, s - 4

                def attn_t_copy(half):
                    wait(act, attn_t_ready, count(i, d, 2) - 1 + half)
                    nc.scalar.copy(attn_t[:, d % 2, 2 * half:2 * half + 2, :, :].rearrange("p b g n -> p (b g n)"),
                                   t_bank[:, :]).then_inc(attn_t_copied, 1)

                def exponentials(g):
                    for b in range(GROUP):
                        last = nc.scalar.activation(
                            attn[:, c % ATTN_RING, g, b, :], s_bank[g][:, b * N:(b + 1) * N], ACT.Exp,
                            bias=neg_max[:, c % 2, g, b:b + 1], scale=1.0,
                            accum_out=row_sum[:, c % 2, g, b:b + 1])
                    last.then_inc(exp_done, 1)

                if exists(i, e):
                    wait(act, o_ready, count(i, e))
                    wait(act, out_stored[e % 2], uses(i, e - 2, 2, 16))
                    nc.scalar.copy(o_sb[:, e % 2, :, :].rearrange("p b a -> p (b a)"), o_bank[:, :]).then_inc(o_copied, 1)
                if exists(i, d):
                    attn_t_copy(0)
                if exists(i, u):
                    wait(act, xt_ready, count(i, u))
                    nc.scalar.copy(xt[:, u % XT_RING, :, :].rearrange("p b f -> p (b f)"),
                                   misc_bank[:, :]).then_inc(xt_copied, 1)
                    nc.scalar.copy(xt_hi[:, u % XT_RING, :, :].rearrange("p b f -> p (b f)"),
                                   misc_bank[:, :]).then_inc(xt_hi_ready, 1)
                if exists(i, d):
                    attn_t_copy(1)
                if exists(i, c):
                    for g in range(NH):
                        wait(act, max_ready, count(i, c, 2) - 1 + g)
                        exponentials(g)
                if s % SPAN == 0 and exists(i, s):
                    wait(act, u_max_ready, spans(i, s))
                    for h in range(NH):
                        nc.scalar.activation(u_exp[:, h, :], misc_bank[0:SPAN_BS, h * F:(h + 1) * F], ACT.Exp,
                                             bias=u_neg_max[:, h:h + 1], scale=1.0,
                                             accum_out=u_sum[:, h:h + 1]).then_inc(u_exp_done, 1)

            steps(act, step, -SPAN, GROUPS + 4)

        @block.vector
        def _(dve):
            dve.wait_ge(weights_loaded, 16 * WEIGHT_DMAS)
            dve.wait_ge(weights_turned, 2)
            wt = misc_bank[:, :].rearrange("p (w a) -> p w a", w=4)
            nc.vector.tensor_scalar(wqk[:, QUERY, :], wt[:, 0, :], INV_SQRT, None, ALU.mult).then_inc(constant_step, 1)
            nc.vector.tensor_copy(wqk[:, KEY, :], wt[:, 1, :]).then_inc(constant_step, 1)
            nc.vector.tensor_copy(wvu[:, 0:A], wt[:, 2, :]).then_inc(constants_ready, 1)
            nc.vector.tensor_copy(wr[:, :], wt[:, 3, :]).then_inc(constants_ready, 1)
            nc.vector.tensor_copy(wvu[:, A:VU], vu_banks[:, 0:NH]).then_inc(constants_ready, 1)
            nc.vector.tensor_tensor(b_centred[:, :], b_own[:, :], b_other[:, :], ALU.subtract).then_inc(constant_step, 1)
            dve.wait_ge(constant_step, 3)
            nc.vector.tensor_scalar(b_centred[:, QUERY:KEY], b_centred[:, QUERY:KEY], INV_SQRT / NH, None,
                                    ALU.mult).then_inc(constants_ready, 1)
            nc.vector.tensor_scalar(b_centred[:, KEY:], b_centred[:, KEY:], 1.0 / NH, None, ALU.mult).then_inc(constants_ready, 1)
            nc.vector.tensor_copy(wqk_hi[:, :, :], wqk[:, :, :]).then_inc(constant_step, 1)
            for r in range(2):
                nc.vector.tensor_tensor(w_mean[:, :, r, :], wqk[:, :, 0:DPH], wqk[:, :, DPH:A], ALU.add).then_inc(constant_step, 1)
            dve.wait_ge(constant_step, 6)
            nc.vector.tensor_tensor(wqk_lo[:, :, :], wqk[:, :, :], wqk_hi[:, :, :].bitcast(F32), ALU.subtract).then_inc(constants_ready, 1)
            for r in range(2):
                nc.vector.tensor_scalar(w_mean[:, :, r, :], w_mean[:, :, r, :], 1.0 / N, None, ALU.mult).then_inc(constants_ready, 1)
            dve.wait_ge(constants_ready, CONSTANTS)

            def step(i, s):
                u, c = s + SPAN, s - 1
                here = slice(s % SPAN * GROUP, (s % SPAN + 1) * GROUP)

                def centre(which, psum, ready, place, copied):
                    wait(dve, ready, count(i, s))
                    by_g = psum[:, :].rearrange("p (b g f) -> p b g f", b=GROUP, g=NH)
                    for h in range(NH):
                        rows = slice(h * DPH, (h + 1) * DPH)
                        for g in range(NH):
                            last = nc.vector.tensor_tensor(
                                place[g * DPH:(g + 1) * DPH, s % 2, :, h * FH:(h + 1) * FH], by_g[rows, :, g, :],
                                offset[rows, which, g, here].unsqueeze(2).broadcast_to([DPH, GROUP, FH]), ALU.add)
                    last.then_inc(copied, 1)

                def values():
                    wait(dve, vu_ready, count(i, u))
                    by_bank = vu_banks[:, :].rearrange("p (k n) -> p k n", k=2)[:, :, 0:2 * VU].rearrange(
                        "p k (b v) -> p k b v", b=2)
                    nc.vector.tensor_tensor(
                        u_logit[:, here, :].rearrange("p (k b) h -> p k b h", k=2), by_bank[:, :, :, A:VU],
                        bvu[:, A:VU].unsqueeze(1).unsqueeze(1).broadcast_to([F, 2, 2, NH]), ALU.add)
                    for g in range(NH):
                        rows = slice(g * FH, (g + 1) * FH)
                        for h in range(NH):
                            cols = slice(h * DPH, (h + 1) * DPH)
                            last = nc.vector.tensor_tensor(
                                v[h * FH:(h + 1) * FH, u % V_RING, :, g, :].rearrange("p (k b) d -> p k b d", k=2),
                                by_bank[rows, :, :, cols],
                                bvu[rows, cols].unsqueeze(1).unsqueeze(1).broadcast_to([FH, 2, 2, DPH]), ALU.add)
                    last.then_inc(vu_copied, 1)

                def inverse(g):
                    wait(dve, exp_done, count(i, c, 2) - 1 + g)
                    nc.vector.reciprocal(row_inv[:, c % 2, g, :], row_sum[:, c % 2, g, :]).then_inc(inv_ready, 1)

                if exists(i, s):
                    wait(dve, offset_ready, spans(i, s))
                    centre(QUERY, qk_bank, q_ready, qs, q_copied)
                if s % SPAN == 1 and exists(i, c):
                    wait(dve, u_exp_done, spans(i, c, 2))
                    nc.vector.reciprocal(u_inv[:, :], u_sum[:, :]).then_inc(u_inv_ready, 1)
                    wait(dve, u_inv_ready, spans(i, c))
                    nc.vector.tensor_tensor(
                        u_soft[:, :, :, :].rearrange("p g h f -> p h g f"),
                        u_exp[:, :, :].rearrange("p h (g f) -> p h g f", g=NH),
                        u_inv[:, :].unsqueeze(2).unsqueeze(3).broadcast_to([SPAN_BS, NH, NH, FH]), ALU.mult,
                    ).then_inc(u_soft_ready, 1)
                if exists(i, u):
                    wait(dve, xt_copied, count(i, u))
                    nc.vector.tensor_reduce(xsum[:, :, here].rearrange("p g b -> p b g"),
                                            xt[:, u % XT_RING, :, :].rearrange("p b (g f) -> p b g f", g=NH),
                                            AX.X, ALU.add).then_inc(xsum_ready, 1)
                if exists(i, c):
                    wait(dve, s_ready, count(i, c))
                    for g in range(NH):
                        nc.vector.tensor_reduce(neg_max[:, c % 2, g, :],
                                                s_bank[g][:, :].rearrange("p (b n) -> p b n", b=GROUP),
                                                AX.X, ALU.max, negate=True).then_inc(max_ready, 1)
                if exists(i, s):
                    centre(KEY, qk_bank, k_ready, ks, k_copied)
                if s % SPAN == 0 and exists(i, s):
                    wait(dve, u_turned, spans(i, s))
                    nc.vector.tensor_reduce(
                        u_neg_max[:, :],
                        misc_bank[0:SPAN_BS, 0:NH * F].rearrange("p (h n) -> p h n", h=NH),
                        AX.X, ALU.max, negate=True).then_inc(u_max_ready, 1)
                if s % SPAN == 1 and exists(i, c):
                    wait(dve, unary_turned, spans(i, c))
                    nc.vector.tensor_copy(unary[:, c // SPAN % 2, :, :],
                                          misc_bank[:, 0:NH * SPAN_BS].rearrange("p (g b) -> p g b", g=NH)
                                          ).then_inc(unary_copied, 1)
                if s % SPAN == SPAN - 1 and exists(i, s + 1):
                    wait(dve, mean_ready, spans(i, s + 1))
                    wait(dve, k_copied, count(i, s))
                    nc.vector.tensor_tensor(
                        offset[:, :, :, :].rearrange("p w g b -> p w (g b)"),
                        b_centred[:, :].unsqueeze(2).broadcast_to([A, 2, NH * SPAN_BS]),
                        misc_bank[:, 0:2 * NH * SPAN_BS].rearrange("p (w n) -> p w n", w=2),
                        ALU.subtract).then_inc(offset_ready, 1)
                if exists(i, u):
                    values()
                if exists(i, c):
                    inverse(0)
                    inverse(1)

            steps(dve, step, -SPAN, GROUPS + 1)

        @block.tensor
        def _(pe):
            soft_count = pe.alloc_register("soft_count")
            pe.reg_mov(soft_count, spans(1, 0))
            pe.wait_ge(ident_ready, 1)
            pe.wait_ge(weights_loaded, 16 * WEIGHT_DMAS)
            for n in range(4):
                last = nc.tensor.transpose(misc_bank[:, n * A:(n + 1) * A], w_rows[:, n, :], ident[:, :])
            last.then_inc(weights_turned, 1)
            nc.tensor.transpose(vu_banks[:, 0:NH], wu_rows[:, :], ident[0:NH, 0:NH]).then_inc(weights_turned, 1)
            pe.wait_ge(constants_ready, CONSTANTS)

            def step(i, s):
                u, c, d = s + SPAN, s - 1, s - 3
                j = s % SPAN

                def half_rows(g):
                    return slice(g * DPH, (g + 1) * DPH)

                def means():
                    wait(pe, xsum_ready, count(i, u))
                    wait(pe, xt_hi_ready, count(i, u))
                    for which in (QUERY, KEY):
                        last = nc.tensor.matmul(
                            misc_bank[:, which * NH * SPAN_BS:(which + 1) * NH * SPAN_BS],
                            w_mean[:, which, :, :].rearrange("p r d -> p (r d)"),
                            xsum[:, :, :].rearrange("p g b -> p (g b)"), start=True, stop=True)
                    last.then_inc(mean_ready, 1)

                def project(which, psum, ready):
                    hi, lo = (x[:, s % XT_RING, :, :].rearrange("p b f -> p (b f)") for x in (xt_hi, xt_lo))
                    nc.tensor.matmul(psum[:, :], wqk_lo[:, which, :], hi, start=True, stop=False)
                    nc.tensor.matmul(psum[:, :], wqk_hi[:, which, :], lo, start=False, stop=False)
                    nc.tensor.matmul(psum[:, :], wqk_hi[:, which, :], hi, start=False, stop=True).then_inc(ready, 1)

                def turn_x():
                    wait(pe, x_loaded[u % X_RING], uses(i, u, X_RING, 16))
                    wait(pe, xt_hi_ready, count(i, u - 1))
                    if j == 0:
                        wait(pe, offset_ready, spans(i, s))
                    if j == 1 and exists(i, c):
                        wait(pe, u_exp_done, spans(i, c, 2))
                    if j == 2 and exists(i, s):
                        wait(pe, unary_copied, spans(i, s))
                    for b in range(GROUP):
                        last = nc.tensor.transpose(misc_bank[:, b * F:(b + 1) * F], x_in[:, u % X_RING, b, :], ident[:, :])
                    last.then_inc(xt_ready, 1)

                def scores():
                    wait(pe, q_copied, count(i, c))
                    wait(pe, k_copied, count(i, c))
                    wait(pe, exp_done, count(i, c - 1, 2))
                    for b in range(GROUP):
                        for g in range(NH):
                            last = nc.tensor.matmul(s_bank[g][:, b * N:(b + 1) * N], qs[half_rows(g), c % 2, b, :],
                                                    ks[half_rows(g), c % 2, b, :], start=True, stop=True)
                    last.then_inc(s_ready, 1)

                def turn_attn(half):
                    wait(pe, attn_t_copied, count(i, d, 2) - 2 + half)
                    for b in range(2):
                        for g in range(NH):
                            at = (b * NH + g) * N
                            last = nc.tensor.transpose(t_bank[:, at:at + N], attn[:, d % ATTN_RING, g, 2 * half + b, :], ident[:, :])
                    last.then_inc(attn_t_ready, 1)

                def values():
                    wait(pe, xt_copied, count(i, u))
                    wait(pe, vu_copied, count(i, u - 1))
                    for b in range(GROUP):
                        at = b // 2 * BANK + b % 2 * VU
                        last = nc.tensor.matmul(vu_banks[:, at:at + VU], xt[:, u % XT_RING, b, :], wvu[:, :],
                                                start=True, stop=True)
                    last.then_inc(vu_ready, 1)

                def residual():
                    wait(pe, o_copied, count(i, d - 1))
                    for b in range(GROUP):
                        nc.tensor.matmul(o_bank[:, b * A:(b + 1) * A], xt[:, d % XT_RING, b, :], wr[:, :],
                                         start=(b == 0), stop=False, skip_group_check=True)

                def weighted(half):
                    wait(pe, attn_t_copied, count(i, d, 2) - 1 + half)
                    for b in range(2 * half, 2 * half + 2):
                        for h in range(NH):
                            for g in range(NH):
                                last = nc.tensor.matmul(
                                    o_bank[g * FH:(g + 1) * FH, b * A + h * DPH:b * A + (h + 1) * DPH],
                                    attn_t[:, d % 2, b, g, h * FH:(h + 1) * FH], v[:, d % V_RING, b, g, :],
                                    start=False, stop=True, skip_group_check=True)
                    if half:
                        last.then_inc(o_ready, 1)

                if exists(i, s):
                    wait(pe, k_copied, count(i, c))
                    wait(pe, xt_lo_ready, count(i, s))
                    project(QUERY, qk_bank, q_ready)
                if exists(i, d):
                    wait(pe, attn_ready, count(i, d, 2))
                    turn_attn(0)
                if exists(i, u):
                    turn_x()
                if exists(i, c):
                    scores()
                if exists(i, d):
                    turn_attn(1)
                if exists(i, s):
                    wait(pe, q_copied, count(i, s))
                    project(KEY, qk_bank, k_ready)
                if exists(i, u):
                    values()
                if exists(i, d):
                    residual()
                if j == 0 and exists(i, s):
                    wait(pe, vu_copied, count(i, s + SPAN - 1))
                    wait(pe, xt_hi_ready, count(i, u) if exists(i, u) else GROUPS)
                    for h in range(NH):
                        last = nc.tensor.transpose(
                            misc_bank[0:SPAN_BS, h * F:(h + 1) * F],
                            u_logit[:, :, h], ident[:, :])
                    last.then_inc(u_turned, 1)
                if j == 1 and exists(i, s):
                    wait(pe, xt_hi_ready, count(i, u) if exists(i, u) else GROUPS)
                    wait_and_step(pe, u_soft_ready, spans(i, s), soft_count, isinstance(i, int))
                    for g in range(NH):
                        last = nc.tensor.transpose(
                            misc_bank[:, g * SPAN_BS:(g + 1) * SPAN_BS],
                            u_soft[:, g, :, :].rearrange("p h f -> p (h f)"), ident[0:SPAN_BS, 0:SPAN_BS])
                    last.then_inc(unary_turned, 1)
                if j == SPAN - 1 and exists(i, u):
                    means()
                if exists(i, d):
                    weighted(0)
                    weighted(1)

            steps(pe, step, -SPAN, GROUPS + 3)


_INS = ['r_inputs', 'L0_rec_unary_w', 'L0_rec_unary_b', 'L0_rec_wq_w', 'L0_rec_wq_b', 'L0_rec_wk_w',
        'L0_rec_wk_b', 'L0_rec_wv_w', 'L0_rec_wv_b', 'L0_rec_res_w', 'L0_rec_res_b']


def kernel(**inputs):
    import numpy as _np
    import concourse.bacc as _bacc
    from concourse import mybir as _mybir
    from concourse.bass_utils import run_bass_kernel_spmd as _run

    nc = _bacc.Bacc("TRN2", target_bir_lowering=False, num_devices=1)
    arrays, args = {}, []
    for name in _INS:
        a = _np.ascontiguousarray(inputs[name])
        arrays[f"in_{name}_dram"] = a
        args.append(nc.dram_tensor(f"in_{name}_dram", a.shape, _mybir.dt.from_np(a.dtype), kind="ExternalInput").ap())
    shape = arrays["in_r_inputs_dram"].shape
    args.append(nc.dram_tensor("out_0_dram", shape, _mybir.dt.float32, kind="ExternalOutput").ap())
    attention_kernel(nc, *args)
    r = _run(nc, [arrays], core_ids=[0])
    return r.results[0]["out_0_dram"]
```
